# Optimizing a Trainium2 kernel written in Bass

```python
import numpy as np
import jax
import jax.numpy as jnp

def _softmax(x, axis=-1):
    return jax.nn.softmax(x, axis=axis)

def _gelu(x):
    return jax.nn.gelu(x, approximate=True)

def _silu(x):
    return jax.nn.silu(x)

def _sigmoid(x):
    return jax.nn.sigmoid(x)

def _layernorm(x, axis=-1, eps=1e-05):
    m = jnp.mean(x, axis=axis, keepdims=True)
    v = jnp.var(x, axis=axis, keepdims=True)
    return (x - m) / jnp.sqrt(v + eps)

def _scatter_add(tgt, idx, src, axis=0):
    return tgt.at[idx].add(src)

def _segment_sum(src, seg, n):
    return jax.ops.segment_sum(src, seg, n)
kernel_name = 'mk_dlrm_tower_d1_rec_r8_6b107f'

def setup_inputs(seed: int=0):
    np.random.seed(seed)
    _w = jnp.asarray

    def _rec_inputs():
        import jax
        import jax.numpy as jnp
        _tk = jax.random.key(seed)
        ids = jnp.stack([jax.random.randint(jax.random.fold_in(_tk, 200 + f), (512,), 0, v, jnp.int32) for f, v in enumerate([125000, 12500, 1000, 12500, 1000, 1250, 1000, 12500, 1250, 1250, 12500, 1250, 1250, 1000, 1000, 1250, 1250, 1000, 1000, 12500, 1250, 12500, 12500, 1000, 1000, 1250])], axis=1)
        tbl_0 = 0.05 * jax.random.normal(jax.random.fold_in(_tk, 500 + 0), (125000, 128), jnp.float32)
        tbl_1 = 0.05 * jax.random.normal(jax.random.fold_in(_tk, 500 + 1), (12500, 128), jnp.float32)
        tbl_2 = 0.05 * jax.random.normal(jax.random.fold_in(_tk, 500 + 2), (1000, 128), jnp.float32)
        tbl_3 = 0.05 * jax.random.normal(jax.random.fold_in(_tk, 500 + 3), (12500, 128), jnp.float32)
        tbl_4 = 0.05 * jax.random.normal(jax.random.fold_in(_tk, 500 + 4), (1000, 128), jnp.float32)
        tbl_5 = 0.05 * jax.random.normal(jax.random.fold_in(_tk, 500 + 5), (1250, 128), jnp.float32)
        tbl_6 = 0.05 * jax.random.normal(jax.random.fold_in(_tk, 500 + 6), (1000, 128), jnp.float32)
        tbl_7 = 0.05 * jax.random.normal(jax.random.fold_in(_tk, 500 + 7), (12500, 128), jnp.float32)
        tbl_8 = 0.05 * jax.random.normal(jax.random.fold_in(_tk, 500 + 8), (1250, 128), jnp.float32)
        tbl_9 = 0.05 * jax.random.normal(jax.random.fold_in(_tk, 500 + 9), (1250, 128), jnp.float32)
        tbl_10 = 0.05 * jax.random.normal(jax.random.fold_in(_tk, 500 + 10), (12500, 128), jnp.float32)
        tbl_11 = 0.05 * jax.random.normal(jax.random.fold_in(_tk, 500 + 11), (1250, 128), jnp.float32)
        tbl_12 = 0.05 * jax.random.normal(jax.random.fold_in(_tk, 500 + 12), (1250, 128), jnp.float32)
        tbl_13 = 0.05 * jax.random.normal(jax.random.fold_in(_tk, 500 + 13), (1000, 128), jnp.float32)
        tbl_14 = 0.05 * jax.random.normal(jax.random.fold_in(_tk, 500 + 14), (1000, 128), jnp.float32)
        tbl_15 = 0.05 * jax.random.normal(jax.random.fold_in(_tk, 500 + 15), (1250, 128), jnp.float32)
        tbl_16 = 0.05 * jax.random.normal(jax.random.fold_in(_tk, 500 + 16), (1250, 128), jnp.float32)
        tbl_17 = 0.05 * jax.random.normal(jax.random.fold_in(_tk, 500 + 17), (1000, 128), jnp.float32)
        tbl_18 = 0.05 * jax.random.normal(jax.random.fold_in(_tk, 500 + 18), (1000, 128), jnp.float32)
        tbl_19 = 0.05 * jax.random.normal(jax.random.fold_in(_tk, 500 + 19), (12500, 128), jnp.float32)
        tbl_20 = 0.05 * jax.random.normal(jax.random.fold_in(_tk, 500 + 20), (1250, 128), jnp.float32)
        tbl_21 = 0.05 * jax.random.normal(jax.random.fold_in(_tk, 500 + 21), (12500, 128), jnp.float32)
        tbl_22 = 0.05 * jax.random.normal(jax.random.fold_in(_tk, 500 + 22), (12500, 128), jnp.float32)
        tbl_23 = 0.05 * jax.random.normal(jax.random.fold_in(_tk, 500 + 23), (1000, 128), jnp.float32)
        tbl_24 = 0.05 * jax.random.normal(jax.random.fold_in(_tk, 500 + 24), (1000, 128), jnp.float32)
        tbl_25 = 0.05 * jax.random.normal(jax.random.fold_in(_tk, 500 + 25), (1250, 128), jnp.float32)
        _rk = jax.random.fold_in(_tk, 7)
        r_dense_features = -0.000520686 + 1.00062 * jax.random.normal(jax.random.fold_in(_rk, 101), (512, 128), jnp.float32)
        W_top1 = 0.0405887 * jax.random.normal(jax.random.fold_in(_tk, 801), (607, 512), jnp.float32)
        W_top2 = 0.0441942 * jax.random.normal(jax.random.fold_in(_tk, 802), (512, 256), jnp.float32)
        W_top3 = 0.0625 * jax.random.normal(jax.random.fold_in(_tk, 803), (256, 1), jnp.float32)
        b_top1 = jnp.zeros((512,), jnp.float32)
        b_top2 = jnp.zeros((256,), jnp.float32)
        return (r_dense_features, ids, tbl_0, tbl_1, tbl_2, tbl_3, tbl_4, tbl_5, tbl_6, tbl_7, tbl_8, tbl_9, tbl_10, tbl_11, tbl_12, tbl_13, tbl_14, tbl_15, tbl_16, tbl_17, tbl_18, tbl_19, tbl_20, tbl_21, tbl_22, tbl_23, tbl_24, tbl_25, W_top1, b_top1, W_top2, b_top2, W_top3)
    r_dense_features, ids, tbl_0, tbl_1, tbl_2, tbl_3, tbl_4, tbl_5, tbl_6, tbl_7, tbl_8, tbl_9, tbl_10, tbl_11, tbl_12, tbl_13, tbl_14, tbl_15, tbl_16, tbl_17, tbl_18, tbl_19, tbl_20, tbl_21, tbl_22, tbl_23, tbl_24, tbl_25, W_top1, b_top1, W_top2, b_top2, W_top3 = _rec_inputs()

    def _L0_rec_setup():
        import jax, jax.numpy as jnp
        import numpy as np
        B, F, D = (2048, 26, 128)
        key = jax.random.key(seed)
        k1, k2 = jax.random.split(key)
        dense_features = jax.random.normal(k1, (B, D), dtype=jnp.float32)
        sparse_values = jax.random.normal(k2, (B, F, D), dtype=jnp.float32)
        return {'dense_features': dense_features, 'sparse_values': sparse_values}
    _L0_rec_all = _L0_rec_setup()
    _L0_rec_in = {k: v for k, v in _L0_rec_all.items() if k in ()}
    del _L0_rec_all
    return {'r_dense_features': r_dense_features, 'ids': ids, 'tbl_0': tbl_0, 'tbl_1': tbl_1, 'tbl_2': tbl_2, 'tbl_3': tbl_3, 'tbl_4': tbl_4, 'tbl_5': tbl_5, 'tbl_6': tbl_6, 'tbl_7': tbl_7, 'tbl_8': tbl_8, 'tbl_9': tbl_9, 'tbl_10': tbl_10, 'tbl_11': tbl_11, 'tbl_12': tbl_12, 'tbl_13': tbl_13, 'tbl_14': tbl_14, 'tbl_15': tbl_15, 'tbl_16': tbl_16, 'tbl_17': tbl_17, 'tbl_18': tbl_18, 'tbl_19': tbl_19, 'tbl_20': tbl_20, 'tbl_21': tbl_21, 'tbl_22': tbl_22, 'tbl_23': tbl_23, 'tbl_24': tbl_24, 'tbl_25': tbl_25, 'W_top1': W_top1, 'b_top1': b_top1, 'W_top2': W_top2, 'b_top2': b_top2, 'W_top3': W_top3}

def reference(r_dense_features, ids, tbl_0, tbl_1, tbl_2, tbl_3, tbl_4, tbl_5, tbl_6, tbl_7, tbl_8, tbl_9, tbl_10, tbl_11, tbl_12, tbl_13, tbl_14, tbl_15, tbl_16, tbl_17, tbl_18, tbl_19, tbl_20, tbl_21, tbl_22, tbl_23, tbl_24, tbl_25, W_top1, b_top1, W_top2, b_top2, W_top3):
    import jax
    import jax.numpy as jnp

    def _L0_rec_ref(dense_features, sparse_values):
        import jax, jax.numpy as jnp
        import numpy as np
        B, F, D = (2048, 26, 128)
        sd = jnp.einsum('bfd,bd->bf', sparse_values, dense_features)
        ss = jnp.einsum('bfd,bgd->bfg', sparse_values, sparse_values)
        iu, ju = jnp.triu_indices(F, k=1)
        pairs = ss[:, iu, ju]
        return jnp.concatenate([dense_features, sd, pairs], axis=1)
    e = jnp.stack([tbl_0[ids[:, 0]], tbl_1[ids[:, 1]], tbl_2[ids[:, 2]], tbl_3[ids[:, 3]], tbl_4[ids[:, 4]], tbl_5[ids[:, 5]], tbl_6[ids[:, 6]], tbl_7[ids[:, 7]], tbl_8[ids[:, 8]], tbl_9[ids[:, 9]], tbl_10[ids[:, 10]], tbl_11[ids[:, 11]], tbl_12[ids[:, 12]], tbl_13[ids[:, 13]], tbl_14[ids[:, 14]], tbl_15[ids[:, 15]], tbl_16[ids[:, 16]], tbl_17[ids[:, 17]], tbl_18[ids[:, 18]], tbl_19[ids[:, 19]], tbl_20[ids[:, 20]], tbl_21[ids[:, 21]], tbl_22[ids[:, 22]], tbl_23[ids[:, 23]], tbl_24[ids[:, 24]], tbl_25[ids[:, 25]]], axis=1)
    z = _L0_rec_ref(r_dense_features, e)
    z = z.reshape(z.shape[0], -1)
    h = jnp.concatenate([z, r_dense_features], axis=1)
    h = jnp.maximum(h @ W_top1 + b_top1, 0.0)
    h = jnp.maximum(h @ W_top2 + b_top2, 0.0)
    y = h @ W_top3
    return y

_drawn_inputs = setup_inputs


def setup_inputs(seed=0):
    import zlib

    import numpy as np

    out = dict(_drawn_inputs(seed))
    spreads = {'b_top1': (0.0, 0.1), 'b_top2': (0.0, 0.1)}
    factors = {}
    for name, (base, spread) in spreads.items():
        noise = np.random.default_rng([zlib.crc32(name.encode()), seed]).standard_normal(out[name].shape)
        drawn = base * np.exp(spread * noise) if base else spread * noise
        out[name] = jnp.asarray(drawn.astype(out[name].dtype))
    for name, factor in factors.items():
        out[name] = (out[name] * factor).astype(out[name].dtype)
    return out
```

```python
from contextlib import ExitStack

import numpy as np

import concourse.bass as bass
from concourse import mybir

F32 = mybir.dt.float32
F32R = mybir.dt.float32r
I32 = mybir.dt.int32
ALU = mybir.AluOpType
ACT = mybir.ActivationFunctionType

P = 128
BATCH, DIM, FIELDS = 512, 128, 26
TILES = BATCH // P
SLOTS = FIELDS + 1
HALF = (SLOTS - 1) // 2
H1, H2 = 512, 256

ONEHOT = [2, 4, 6, 13, 14, 17, 18, 23]
GATHERED = [f for f in range(FIELDS) if f not in ONEHOT]
NOH = len(ONEHOT)
FIXED = 1 + NOH
OH_ROWS = 1000
OH_PART = 125
OH_CH = OH_ROWS // OH_PART
DVE_CH = OH_CH - 1
GROUP = 3
GROUPS = len(GATHERED) // GROUP
assert GROUPS * GROUP == len(GATHERED) and GROUPS % 2 == 0 and SLOTS % 2 == 1

ZCH = 3
ZF = SLOTS // ZCH
ZK = ZF * HALF
ETS = SLOTS + 1
BLK = 32
QUADS = P // BLK
NT1, NT2 = H1 // P, H2 // P


def slot_fields():
    return [0] + [1 + f for f in ONEHOT] + [1 + f for f in GATHERED]


def w1_pair_rows():
    of = slot_fields()
    rows = []
    for f in range(SLOTS):
        for step in range(1, HALF + 1):
            a, b = sorted((of[f], of[(f + step) % SLOTS]))
            if a == 0:
                rows.append(DIM + b - 1)
            else:
                i, j = a - 1, b - 1
                rows.append(DIM + FIELDS + i * FIELDS - i * (i + 1) // 2 + j - i - 1)
    return rows


def dlrm_tower(nc, ids, ids_oh, dense_t, oh_tables, tables, w1_pairs, w1_dense, w2, w3, b1, b2, ident, rows, out):
    ctx = ExitStack()
    with ctx:
        def sb(name, shape, dt=F32):
            return ctx.enter_context(nc.sbuf_tensor(name, shape, dt))

        def psum(name, shape):
            return ctx.enter_context(nc.psum_tensor(name, shape, F32))

        def sem(name):
            return ctx.enter_context(nc.semaphore(name))

        ids_sb = sb("ids_sb", [P, TILES * FIELDS], I32)
        ids_bc = sb("ids_bc", [OH_PART, NOH, BATCH], I32)
        ident_sb = sb("ident_sb", [P, P])
        rows_sb = sb("rows_sb", [OH_PART, OH_CH + 2])
        raw = sb("raw", [OH_PART, 2, OH_CH * DIM])
        hi = sb("hi", [OH_PART, 2, OH_CH, DIM], F32R)
        lo = sb("lo", [OH_PART, 2, OH_CH, DIM], F32R)
        onehot = sb("onehot", [OH_PART, 2, OH_CH, BATCH], F32R)
        dist = sb("dist", [OH_PART, 2, BATCH])
        fixed = sb("fixed", [P, FIXED, BATCH])
        got = sb("got", [P, len(GATHERED), DIM])
        vecs = sb("vecs", [P, P, ETS])
        zfull = sb("zfull", [P, SLOTS + HALF, BLK])
        pairs = sb("pairs", [P, SLOTS, HALF])
        zt = sb("zt", [ZK, ZCH, P])
        w1p_sb = sb("w1p_sb", [ZK, ZCH, H1])
        w1d_sb = sb("w1d_sb", [P, 2, H1])
        w1s_sb = sb("w1s_sb", [P, H1])
        w2_sb = sb("w2_sb", [P, NT1, H2])
        w3_sb = sb("w3_sb", [P, NT2])
        b1_sb = sb("b1_sb", [P, NT1])
        b2_sb = sb("b2_sb", [P, NT2])
        h1 = sb("h1", [P, NT1, P])
        h2 = sb("h2", [P, NT2, P])
        y_sb = sb("y_sb", [P, TILES])

        turn_ps = [psum(f"turn_ps{i}", [P, 512]) for i in range(2)]
        gram_ps = psum("gram_ps", [P, BLK, BLK])
        zt_ps = psum("zt_ps", [P, 512])
        h1_ps = [psum(f"h1_ps{i}", [P, 512]) for i in range(2)]
        h2_ps = psum("h2_ps", [P, 512])
        y_ps = h2_ps[:, 2 * P:2 * P + 1]

        ids_in = sem("ids_in")
        rows_in = sem("rows_in")
        bc_in = [sem("bc_first_in"), sem("bc_rest_in")]
        table_in = [sem(f"table_in{i}") for i in range(2)]
        ident_in = sem("ident_in")
        dense_in = sem("dense_in")
        weights_in = sem("weights_in")
        gathered = [sem(f"gathered{i}") for i in range(GROUPS)]
        hi_ready = sem("hi_ready")
        lo_ready = sem("lo_ready")
        oh_dve = sem("oh_dve")
        dist_ready = sem("dist_ready")
        oh_act = sem("oh_act")
        looked_up = sem("looked_up")
        fixed_ready = sem("fixed_ready")
        turned = sem("turned")
        vecs_fixed = sem("vecs_fixed")
        vecs_moved = sem("vecs_moved")
        gram_cleared = sem("gram_cleared")
        gram_done = sem("gram_done")
        z_ready = sem("z_ready")
        pairs_ready = sem("pairs_ready")
        zt_done = sem("zt_done")
        zt_ready = sem("zt_ready")
        w1_summed = sem("w1_summed")
        h1_done = sem("h1_done")
        h1a_ready = sem("h1a_ready")
        h1b_ready = sem("h1b_ready")
        h2_done = sem("h2_done")
        h2_ready = sem("h2_ready")
        y_done = sem("y_done")
        y_ready = sem("y_ready")
        out_done = sem("out_done")

        block = ctx.enter_context(nc.Block())

        @block.sync
        def _(sp):
            sp.dma_start(ids_sb[:], ids).then_inc(ids_in, 16)
            sp.dma_start(ids_bc[:, 0, :], ids_oh[0:1, :].to_broadcast([OH_PART, BATCH])).then_inc(bc_in[0], 16)
            for j in range(2):
                sp.dma_start(raw[:, j, :], oh_tables[j]).then_inc(table_in[j], 16)
            sp.dma_start(ids_bc[:, 1:, :].rearrange("p k b -> p (k b)"),
                         ids_oh[1:, :].rearrange("(o k) b -> o (k b)", o=1).to_broadcast(
                             [OH_PART, (NOH - 1) * BATCH])).then_inc(bc_in[1], 16)
            for j in range(2, NOH):
                sp.wait_ge(lo_ready, j - 1)
                sp.dma_start(raw[:, j % 2, :], oh_tables[j]).then_inc(table_in[j % 2], 16)
            sp.wait_ge(y_ready, TILES)
            sp.dma_start(out, y_sb[:]).then_inc(out_done, 16)
            sp.wait_ge(out_done, 16)

        @block.gpsimd
        def _(pool):
            pool.wait_ge(ids_in, 16)
            for t in range(TILES):
                for k, f in enumerate(GATHERED):
                    if t > 0 and k % GROUP == 0:
                        pool.wait_ge(turned, GROUPS * (t - 1) + k // GROUP + 1)
                    at = t * FIELDS + f
                    nc.gpsimd.indirect_dma_start(
                        out=got[:, k, :], out_offset=None, in_=tables[k],
                        in_offset=bass.IndirectOffsetOnAxis(ap=ids_sb[:, at:at + 1], axis=0),
                    ).then_inc(gathered[k // GROUP], 16)

        @block.scalar
        def _(act):
            act.dma_start(rows_sb[:], rows).then_inc(rows_in, 16)
            act.dma_start(ident_sb[:], ident).then_inc(ident_in, 16)
            act.dma_start(fixed[:, 0, :], dense_t).then_inc(dense_in, 16)
            act.dma_start(w1p_sb[:], w1_pairs).then_inc(weights_in, 16)
            act.dma_start(w1d_sb[:], w1_dense).then_inc(weights_in, 16)
            act.dma_start(w2_sb[:], w2).then_inc(weights_in, 16)
            act.dma_start(w3_sb[:], w3).then_inc(weights_in, 16)
            act.dma_start(b1_sb[:], b1).then_inc(weights_in, 16)
            act.dma_start(b2_sb[:], b2).then_inc(weights_in, 16)

            def look_up(j):
                if j < NOH:
                    act.wait_ge(table_in[j % 2], 16 * (j // 2 + 1))
                    if j >= 2:
                        act.wait_ge(looked_up, j - 1)
                    nc.scalar.activation(hi[:, j % 2].rearrange("p c d -> p (c d)"), raw[:, j % 2, :],
                                         ACT.Copy).then_inc(hi_ready, 1)
                    act.wait_ge(bc_in[min(j, 1)], 16)
                    act.wait_ge(rows_in, 16)
                    if j >= 2:
                        act.wait_ge(oh_act, j - 1)
                    nc.scalar.activation(dist[:, j % 2, :], ids_bc[:, j, :], ACT.Square,
                                         bias=rows_sb[:, OH_CH:OH_CH + 1]).then_inc(dist_ready, 1)
                    act.wait_ge(dist_ready, j + 1)
                    nc.scalar.activation(onehot[:, j % 2, OH_CH - 1, :], dist[:, j % 2, :], ACT.Relu,
                                         bias=rows_sb[:, OH_CH + 1:OH_CH + 2], scale=-1.0).then_inc(oh_act, 1)
                if j >= 1:
                    act.wait_ge(looked_up, j)
                    nc.scalar.activation(fixed[:, j, :], h1_ps[(j - 1) % 2][:, 0:BATCH],
                                         ACT.Copy).then_inc(fixed_ready, 1)

            def move_group(t, i):
                act.wait_ge(turned, GROUPS * t + i + 1)
                nc.scalar.activation(
                    vecs[:, :, FIXED + GROUP * i:FIXED + GROUP * (i + 1)].rearrange("d b s -> d s b"),
                    turn_ps[i % 2][:, 0:GROUP * P].rearrange("d (s b) -> d s b", s=GROUP),
                    ACT.Copy).then_inc(vecs_moved, 1)

            def move_fixed(t):
                nc.scalar.activation(vecs[:, :, 0:FIXED].rearrange("d b s -> d s b"),
                                     fixed[:, :, bass.ds(t * P, P)], ACT.Copy).then_inc(vecs_fixed, 1)

            def relu_h1a(t):
                act.wait_ge(h1_done, 2 * t + 1)
                if not (isinstance(t, int) and t == 0):
                    act.wait_ge(h2_done, t)
                for n in range(NT1 // 2):
                    nc.scalar.activation(h1[:, n, :], h1_ps[0][:, n * P:(n + 1) * P], ACT.Relu,
                                         bias=b1_sb[:, n:n + 1]).then_inc(h1a_ready, 1)

            def relu_h2(t):
                act.wait_ge(h2_done, t + 1)
                if not (isinstance(t, int) and t == 0):
                    act.wait_ge(y_done, t)
                for n in range(NT2):
                    nc.scalar.activation(h2[:, n, :], h2_ps[:, n * P:(n + 1) * P], ACT.Relu,
                                         bias=b2_sb[:, n:n + 1]).then_inc(h2_ready, 1)

            def move_y(t):
                act.wait_ge(y_done, t + 1)
                nc.scalar.activation(y_sb[:, bass.ds(t, 1)], y_ps, ACT.Copy).then_inc(y_ready, 1)

            first_groups = {2: [0], 4: [1, 2], 6: [3, 4, 5]}
            for j in range(NOH + 1):
                look_up(j)
                for i in first_groups.get(j, []):
                    move_group(0, i)
            act.wait_ge(fixed_ready, NOH)
            act.wait_ge(dense_in, 16)
            move_fixed(0)
            act.wait_ge(weights_in, 6 * 16)
            with act.Fori(1, TILES) as t:
                act.wait_ge(gram_done, t)
                move_fixed(t)
                move_group(t, 0)
                move_group(t, 1)
                move_group(t, 2)
                relu_h1a(t - 1)
                move_group(t, 3)
                relu_h2(t - 1)
                move_group(t, 4)
                move_y(t - 1)
                move_group(t, 5)
            relu_h1a(TILES - 1)
            relu_h2(TILES - 1)
            move_y(TILES - 1)

        @block.vector
        def _(dve):
            nc.vector.memset(gram_ps[:], 0.0).then_inc(gram_cleared, 1)
            for j in range(NOH):
                dve.wait_ge(bc_in[min(j, 1)], 16)
                dve.wait_ge(rows_in, 16)
                if j >= 2:
                    dve.wait_ge(looked_up, j - 1)
                for c in range(DVE_CH):
                    nc.vector.tensor_scalar(onehot[:, j % 2, c, :], ids_bc[:, j, :], rows_sb[:, c:c + 1], None,
                                            ALU.is_equal).then_inc(oh_dve, 1)
                    if c == 1:
                        dve.wait_ge(hi_ready, j + 1)
                        nc.vector.tensor_tensor(lo[:, j % 2].rearrange("p c d -> p (c d)"), raw[:, j % 2, :],
                                                hi[:, j % 2].rearrange("p c d -> p (c d)"),
                                                ALU.subtract).then_inc(lo_ready, 1)
            dve.wait_ge(weights_in, 6 * 16)
            nc.vector.tensor_tensor(w1s_sb[:], w1d_sb[:, 0, :], w1d_sb[:, 1, :], ALU.add).then_inc(w1_summed, 1)

            def tile(t):
                later = not (isinstance(t, int) and t == 0)
                dve.wait_ge(gram_done, t + 1)
                if later:
                    dve.wait_ge(pairs_ready, t)
                nc.vector.transpose(zfull[:, 0:SLOTS, :], gram_ps[:, :, 0:SLOTS].rearrange("q b g -> q g b")
                                    ).then_inc(z_ready, 1)
                nc.vector.transpose(zfull[:, SLOTS:, :], gram_ps[:, :, 0:HALF].rearrange("q b g -> q g b")
                                    ).then_inc(z_ready, 1)
                dve.wait_ge(z_ready, 2 * t + 2)
                if later:
                    dve.wait_ge(zt_done, t)
                z = zfull[:]
                walk = bass.AP(z.tensor, z.offset + BLK, [z.ap[0], [BLK + 1, SLOTS], [BLK, HALF]])
                nc.vector.tensor_copy(pairs[:], walk).then_inc(pairs_ready, 1)
                dve.wait_ge(zt_done, t + 1)
                if later:
                    dve.wait_ge(h1_done, 2 * t)
                nc.vector.tensor_copy(zt[:].rearrange("k c b -> k (c b)"), zt_ps[0:ZK, 0:ZCH * P]
                                      ).then_inc(zt_ready, 1)
                dve.wait_ge(h1_done, 2 * t + 2)
                if later:
                    dve.wait_ge(h2_done, t)
                for n in range(NT1 // 2, NT1):
                    m = n - NT1 // 2
                    nc.vector.tensor_scalar(h1[:, n, :], h1_ps[1][:, m * P:(m + 1) * P], b1_sb[:, n:n + 1], 0.0,
                                            ALU.add, ALU.max).then_inc(h1b_ready, 1)

            tile(0)
            with dve.Fori(1, TILES) as t:
                tile(t)

        @block.tensor
        def _(pe):
            def look_up(j):
                if j >= 2:
                    pe.wait_ge(fixed_ready, j - 1)
                for c in range(OH_CH):
                    if c < DVE_CH:
                        pe.wait_ge(oh_dve, DVE_CH * j + c + 1)
                    else:
                        pe.wait_ge(oh_act, j + 1)
                    if c == 0:
                        pe.wait_ge(hi_ready, j + 1)
                    nc.tensor.matmul(h1_ps[j % 2][:, 0:BATCH], hi[:, j % 2, c, :], onehot[:, j % 2, c, :],
                                     start=(c == 0), stop=False)
                pe.wait_ge(lo_ready, j + 1)
                for c in range(OH_CH):
                    last = nc.tensor.matmul(h1_ps[j % 2][:, 0:BATCH], lo[:, j % 2, c, :], onehot[:, j % 2, c, :],
                                            start=False, stop=(c == OH_CH - 1))
                last.then_inc(looked_up, 1)

            def turn_group(t, i):
                pe.wait_ge(gathered[i], 16 * GROUP * t + 16 * GROUP)
                if not (isinstance(t, int) and t == 0 and i < 2):
                    pe.wait_ge(vecs_moved, GROUPS * t + i - 1)
                for k in range(GROUP):
                    last = nc.tensor.transpose(turn_ps[i % 2][:, k * P:(k + 1) * P], got[:, GROUP * i + k, :],
                                               ident_sb[:])
                last.then_inc(turned, 1)

            def gram(t):
                pe.wait_ge(vecs_fixed, t + 1)
                pe.wait_ge(vecs_moved, GROUPS * t + GROUPS)
                if not (isinstance(t, int) and t == 0):
                    pe.wait_ge(z_ready, 2 * t)
                for b in range(BLK):
                    for j in range(QUADS):
                        v = vecs[:, BLK * j + b, 0:SLOTS]
                        last = nc.tensor.matmul(gram_ps[BLK * j:BLK * j + SLOTS, b, 0:SLOTS], v, v,
                                                start=True, stop=True)
                last.then_inc(gram_done, 1)

            def turn_pairs(t):
                pe.wait_ge(pairs_ready, t + 1)
                if not (isinstance(t, int) and t == 0):
                    pe.wait_ge(zt_ready, t)
                for c in range(ZCH):
                    last = nc.tensor.transpose(zt_ps[0:ZK, c * P:(c + 1) * P],
                                               pairs[:, ZF * c:ZF * (c + 1), :].rearrange("b f s -> b (f s)"),
                                               ident_sb[:])
                last.then_inc(zt_done, 1)

            def layer1(t):
                for n in range(NT1):
                    bank, col = h1_ps[n // 2], (n % 2) * P
                    if n % 2 == 0 and not (isinstance(t, int) and t == 0):
                        pe.wait_ge(h1a_ready if n == 0 else h1b_ready, NT1 // 2 * t)
                    nc.tensor.matmul(bank[:, col:col + P], w1s_sb[:, n * P:(n + 1) * P],
                                     fixed[:, 0, bass.ds(t * P, P)], start=True, stop=False)
                    if n == 0:
                        pe.wait_ge(zt_ready, t + 1)
                    for c in range(ZCH):
                        last = nc.tensor.matmul(bank[:, col:col + P], w1p_sb[:, c, n * P:(n + 1) * P], zt[:, c, :],
                                                start=False, stop=(c == ZCH - 1))
                    if n % 2 == 1:
                        last.then_inc(h1_done, 1)

            def layer2(t):
                if not (isinstance(t, int) and t == 0):
                    pe.wait_ge(y_ready, t)
                for m in range(NT2):
                    for n in range(NT1):
                        if m == 0:
                            half = NT1 // 2
                            pe.wait_ge(h1a_ready if n < half else h1b_ready, half * t + n % half + 1)
                        last = nc.tensor.matmul(h2_ps[:, m * P:(m + 1) * P], w2_sb[:, n, m * P:(m + 1) * P],
                                                h1[:, n, :], start=(n == 0), stop=(n == NT1 - 1))
                last.then_inc(h2_done, 1)

            def layer3(t):
                pe.wait_ge(h2_ready, NT2 * t + NT2)
                for m in range(NT2):
                    last = nc.tensor.matmul(y_ps, h2[:, m, :], w3_sb[:, m:m + 1], start=(m == 0), stop=(m == NT2 - 1))
                last.then_inc(y_done, 1)

            pe.wait_ge(ident_in, 16)
            pe.wait_ge(gram_cleared, 1)
            first_groups = {1: [0], 3: [1, 2], 5: [3, 4, 5]}
            for j in range(NOH):
                look_up(j)
                for i in first_groups.get(j, []):
                    turn_group(0, i)
            gram(0)
            pe.wait_ge(weights_in, 6 * 16)
            pe.wait_ge(w1_summed, 1)
            with pe.Fori(1, TILES) as t:
                turn_group(t, 0)
                turn_group(t, 1)
                turn_pairs(t - 1)
                turn_group(t, 2)
                layer1(t - 1)
                turn_group(t, 3)
                layer2(t - 1)
                turn_group(t, 4)
                layer3(t - 1)
                turn_group(t, 5)
                gram(t)
            turn_pairs(TILES - 1)
            layer1(TILES - 1)
            layer2(TILES - 1)
            layer3(TILES - 1)


def kernel(**inputs):
    import concourse.bacc as bacc
    from concourse.bass_utils import run_bass_kernel_spmd

    a = {k: np.asarray(v) for k, v in inputs.items()}
    ids = a["ids"]
    w1 = a["W_top1"]
    row_of = (OH_CH * np.arange(OH_PART)[:, None] + np.arange(OH_CH)[None, :]).astype(np.float32)
    rows = np.concatenate([row_of, -row_of[:, -1:], np.ones((OH_PART, 1), np.float32)], axis=1)
    arrays = {
        "ids": ids.reshape(P, TILES * FIELDS),
        "ids_oh": np.stack([ids[:, f].reshape(P, TILES).T.reshape(BATCH) for f in ONEHOT]),
        "dense_t": a["r_dense_features"].reshape(P, TILES, DIM).transpose(2, 1, 0).reshape(DIM, BATCH),
        "oh_tables": np.stack([a[f"tbl_{f}"].reshape(OH_PART, OH_CH * DIM) for f in ONEHOT]),
        "w1_pairs": w1[w1_pair_rows()].reshape(ZCH, ZK, H1).transpose(1, 0, 2),
        "w1_dense": np.stack([w1[:DIM], w1[-DIM:]], axis=1),
        "w2": a["W_top2"].reshape(NT1, P, H2).transpose(1, 0, 2),
        "w3": a["W_top3"].reshape(NT2, P).T,
        "b1": a["b_top1"].reshape(NT1, P).T,
        "b2": a["b_top2"].reshape(NT2, P).T,
        "ident": np.eye(P, dtype=np.float32),
        "rows": rows,
    }
    for f in GATHERED:
        arrays[f"tbl_{f}"] = a[f"tbl_{f}"]
    arrays = {k: np.ascontiguousarray(v) for k, v in arrays.items()}

    nc = bacc.Bacc("TRN2", target_bir_lowering=False, num_devices=1)
    d = {k: nc.dram_tensor(k, v.shape, mybir.dt.from_np(v.dtype), kind="ExternalInput").ap()
         for k, v in arrays.items()}
    y = nc.dram_tensor("y", (BATCH, 1), F32, kind="ExternalOutput").ap()
    dlrm_tower(nc, d["ids"], d["ids_oh"], d["dense_t"], [d["oh_tables"][j] for j in range(NOH)],
               [d[f"tbl_{f}"] for f in GATHERED], d["w1_pairs"], d["w1_dense"], d["w2"], d["w3"],
               d["b1"], d["b2"], d["ident"], d["rows"], y.rearrange("(p t) o -> p (t o)", t=TILES))
    r = run_bass_kernel_spmd(nc, [arrays], core_ids=[0])
    return r.results[0]["y"]
```

```python
from contextlib import ExitStack

import numpy as np

import concourse.bass as bass
from concourse import mybir

F32 = mybir.dt.float32
F32R = mybir.dt.float32r
I32 = mybir.dt.int32
ALU = mybir.AluOpType
ACT = mybir.ActivationFunctionType

P = 128
BATCH, DIM, FIELDS = 512, 128, 26
TILES = BATCH // P
SLOTS = FIELDS + 1
HALF = (SLOTS - 1) // 2
H1, H2 = 512, 256

ONEHOT = [2, 4, 6, 13, 14, 17, 18, 23]
GATHERED = [f for f in range(FIELDS) if f not in ONEHOT]
NOH = len(ONEHOT)
FIXED = 1 + NOH
OH_ROWS = 1000
OH_PART = 125
OH_CH = OH_ROWS // OH_PART
DVE_CH = [OH_CH - 1 - j % 2 for j in range(NOH)]
GROUP = [4, 3, 3, 3, 3, 2]
GROUPS = len(GROUP)
GROUP_AT = [sum(GROUP[:i]) for i in range(GROUPS + 1)]
assert GROUP_AT[-1] == len(GATHERED) and GROUPS % 2 == 0 and GROUPS == NOH - 2 and SLOTS % 2 == 1

NEAR = SLOTS - HALF
ZCH = 3
ZF = SLOTS // ZCH
ZK = ZF * HALF
ETS = SLOTS + 1
BLK = 32
QUADS = P // BLK
NT1, NT2 = H1 // P, H2 // P


def slot_fields():
    return [0] + [1 + f for f in ONEHOT] + [1 + f for f in GATHERED]


def w1_pair_rows():
    of = slot_fields()
    rows = []
    for f in range(SLOTS):
        for step in range(1, HALF + 1):
            a, b = sorted((of[f], of[(f + step) % SLOTS]))
            if a == 0:
                rows.append(DIM + b - 1)
            else:
                i, j = a - 1, b - 1
                rows.append(DIM + FIELDS + i * FIELDS - i * (i + 1) // 2 + j - i - 1)
    return rows


def dlrm_tower(nc, ids, ids_oh, dense_t, oh_tables, tables, w1_pairs, w1_dense, w2, w3, b1, b2, ident, rows, out):
    ctx = ExitStack()
    with ctx:
        def sb(name, shape, dt=F32):
            return ctx.enter_context(nc.sbuf_tensor(name, shape, dt))

        def psum(name, shape):
            return ctx.enter_context(nc.psum_tensor(name, shape, F32))

        def sem(name):
            return ctx.enter_context(nc.semaphore(name))

        ids_sb = sb("ids_sb", [P, TILES * FIELDS], I32)
        ids_bc = sb("ids_bc", [OH_PART, NOH, BATCH], I32)
        ident_sb = sb("ident_sb", [P, P])
        rows_sb = sb("rows_sb", [OH_PART, 2 * OH_CH + 1])
        raw = sb("raw", [OH_PART, 2, OH_CH * DIM])
        hi = sb("hi", [OH_PART, 2, OH_CH, DIM], F32R)
        lo = sb("lo", [OH_PART, 2, OH_CH, DIM], F32R)
        onehot = sb("onehot", [OH_PART, 2, OH_CH, BATCH], F32R)
        dist = sb("dist", [OH_PART, BATCH])
        fixed = sb("fixed", [P, FIXED, BATCH])
        got = sb("got", [P, len(GATHERED), DIM])
        vecs = sb("vecs", [P, P, ETS])
        zfull = sb("zfull", [P, SLOTS + HALF, BLK])
        pairs = sb("pairs", [P, SLOTS, HALF])
        zt = sb("zt", [ZK, ZCH, P])
        w1p_sb = sb("w1p_sb", [ZK, ZCH, H1])
        w1d_sb = sb("w1d_sb", [P, 2, H1])
        w1s_sb = sb("w1s_sb", [P, H1])
        w2_sb = sb("w2_sb", [P, NT1, H2])
        w3_sb = sb("w3_sb", [P, NT2])
        b1_sb = sb("b1_sb", [P, NT1])
        b2_sb = sb("b2_sb", [P, NT2])
        h1 = sb("h1", [P, NT1, P])
        h2 = sb("h2", [P, NT2, BATCH])
        y_sb = sb("y_sb", [P, TILES])

        turn_ps = [psum(f"turn_ps{i}", [P, 512]) for i in range(2)]
        gram_ps = psum("gram_ps", [P, BLK, BLK])
        zt_ps = psum("zt_ps", [P, 512])
        h1_ps = [psum(f"h1_ps{i}", [P, 512]) for i in range(2)]
        h2_ps = psum("h2_ps", [P, 512])
        h2_at = [h2_ps[:, 0:P], h1_ps[0][:, 0:P]]
        y_ps = zt_ps[:, ZCH * P:ZCH * P + TILES]

        ids_in = sem("ids_in")
        rows_in = sem("rows_in")
        bc_in = [sem(f"bc_in{j}") for j in range(NOH)]
        table_in = [sem(f"table_in{i}") for i in range(2)]
        ident_in = sem("ident_in")
        dense_in = sem("dense_in")
        weights_in = sem("weights_in")
        gathered = [sem(f"gathered{i}") for i in range(GROUPS)]
        hi_ready = sem("hi_ready")
        lo_ready = sem("lo_ready")
        oh_dve = sem("oh_dve")
        dist_ready = sem("dist_ready")
        oh_act = sem("oh_act")
        looked_up = sem("looked_up")
        fixed_ready = sem("fixed_ready")
        turned = sem("turned")
        vecs_fixed = sem("vecs_fixed")
        vecs_moved = sem("vecs_moved")
        gram_cleared = sem("gram_cleared")
        gram_done = sem("gram_done")
        z_ready = sem("z_ready")
        near_ready = sem("near_ready")
        pairs_ready = sem("pairs_ready")
        zt_done = sem("zt_done")
        zt_ready = sem("zt_ready")
        w1_summed = sem("w1_summed")
        h1_done = sem("h1_done")
        h1a_ready = sem("h1a_ready")
        h1b_ready = sem("h1b_ready")
        h2_done = sem("h2_done")
        h2_ready = sem("h2_ready")
        h2_far_ready = sem("h2_far_ready")
        y_done = sem("y_done")
        y_ready = sem("y_ready")
        out_done = sem("out_done")

        def walk(f0, f1):
            z = zfull[:]
            return bass.AP(z.tensor, z.offset + BLK + (BLK + 1) * f0, [z.ap[0], [BLK + 1, f1 - f0], [BLK, HALF]])

        block = ctx.enter_context(nc.Block())

        @block.sync
        def _(sp):
            sp.dma_start(ids_sb[:], ids).then_inc(ids_in, 16)
            for j in range(NOH):
                if j >= 2:
                    sp.wait_ge(lo_ready, j - 1)
                sp.dma_start(ids_bc[:, j, :], ids_oh[j:j + 1, :].to_broadcast([OH_PART, BATCH])).then_inc(bc_in[j], 16)
                if j >= 1:
                    sp.dma_start(raw[:, j % 2, :], oh_tables[j]).then_inc(table_in[j % 2], 16)
                if j == 1:
                    sp.dma_start(ident_sb[:], ident).then_inc(ident_in, 16)
            sp.dma_start(fixed[:, 0, :], dense_t).then_inc(dense_in, 16)
            for there, here in ((w1p_sb, w1_pairs), (w1d_sb, w1_dense), (w2_sb, w2), (w3_sb, w3), (b1_sb, b1), (b2_sb, b2)):
                sp.dma_start(there[:], here).then_inc(weights_in, 16)
            sp.wait_ge(y_ready, 1)
            sp.dma_start(out, y_sb[:]).then_inc(out_done, 16)
            sp.wait_ge(out_done, 16)

        @block.gpsimd
        def _(pool):
            pool.wait_ge(ids_in, 16)
            for t in range(TILES):
                for i in range(GROUPS):
                    if t > 0:
                        pool.wait_ge(turned, GROUPS * (t - 1) + i + 1)
                    for k in range(GROUP_AT[i], GROUP_AT[i + 1]):
                        at = t * FIELDS + GATHERED[k]
                        nc.gpsimd.indirect_dma_start(
                            out=got[:, k, :], out_offset=None, in_=tables[k],
                            in_offset=bass.IndirectOffsetOnAxis(ap=ids_sb[:, at:at + 1], axis=0),
                        ).then_inc(gathered[i], 16)

        @block.scalar
        def _(act):
            act.dma_start(rows_sb[:], rows).then_inc(rows_in, 16)
            act.dma_start(raw[:, 0, :], oh_tables[0]).then_inc(table_in[0], 16)

            def look_up(j):
                if j < NOH:
                    act.wait_ge(table_in[j % 2], 16 * (j // 2 + 1))
                    if j >= 2:
                        act.wait_ge(looked_up, j - 1)
                    nc.scalar.activation(hi[:, j % 2].rearrange("p c d -> p (c d)"), raw[:, j % 2, :],
                                         ACT.Copy).then_inc(hi_ready, 1)
                    act.wait_ge(bc_in[j], 16)
                    act.wait_ge(rows_in, 16)
                    for c in range(DVE_CH[j], OH_CH):
                        n = sum(OH_CH - m for m in DVE_CH[:j]) + c - DVE_CH[j]
                        if n > 0:
                            act.wait_ge(oh_act, n)
                        nc.scalar.activation(dist[:], ids_bc[:, j, :], ACT.Square,
                                             bias=rows_sb[:, OH_CH + c:OH_CH + c + 1]).then_inc(dist_ready, 1)
                        act.wait_ge(dist_ready, n + 1)
                        nc.scalar.activation(onehot[:, j % 2, c, :], dist[:], ACT.Relu,
                                             bias=rows_sb[:, 2 * OH_CH:], scale=-1.0).then_inc(oh_act, 1)
                if j >= 1:
                    act.wait_ge(looked_up, j)
                    nc.scalar.activation(fixed[:, j, :], h1_ps[(j - 1) % 2][:, 0:BATCH],
                                         ACT.Copy).then_inc(fixed_ready, 1)

            def move_group(t, i):
                act.wait_ge(turned, GROUPS * t + i + 1)
                nc.scalar.activation(
                    vecs[:, :, FIXED + GROUP_AT[i]:FIXED + GROUP_AT[i + 1]].rearrange("d b s -> d s b"),
                    turn_ps[i % 2][:, 0:GROUP[i] * P].rearrange("d (s b) -> d s b", s=GROUP[i]),
                    ACT.Copy).then_inc(vecs_moved, 1)

            def move_fixed(t):
                nc.scalar.activation(vecs[:, :, 0:FIXED].rearrange("d b s -> d s b"),
                                     fixed[:, :, bass.ds(t * P, P)], ACT.Copy).then_inc(vecs_fixed, 1)

            def relu_h1a(t):
                act.wait_ge(h1_done, 2 * t + 1)
                if not (isinstance(t, int) and t == 0):
                    act.wait_ge(h2_done, NT2 * t)
                for n in range(NT1 // 2):
                    nc.scalar.activation(h1[:, n, :], h1_ps[0][:, n * P:(n + 1) * P], ACT.Relu,
                                         bias=b1_sb[:, n:n + 1]).then_inc(h1a_ready, 1)

            def relu_h2(t):
                act.wait_ge(h2_done, NT2 * t + 1)
                nc.scalar.activation(h2[:, 0, bass.ds(t * P, P)], h2_at[0], ACT.Relu, bias=b2_sb[:, 0:1]).then_inc(h2_ready, 1)

            def near_pairs(t):
                act.wait_ge(z_ready, 2 * t + 1)
                if not (isinstance(t, int) and t == 0):
                    act.wait_ge(zt_done, t)
                nc.scalar.activation(pairs[:, 0:NEAR, :], walk(0, NEAR), ACT.Copy).then_inc(near_ready, 1)

            for j in range(NOH):
                look_up(j)
                if j >= 2:
                    move_group(0, j - 2)
            act.wait_ge(fixed_ready, NOH - 1)
            act.wait_ge(dense_in, 16)
            nc.scalar.activation(vecs[:, :, 0:NOH].rearrange("d b s -> d s b"), fixed[:, 0:NOH, 0:P],
                                 ACT.Copy).then_inc(vecs_fixed, 1)
            act.wait_ge(looked_up, NOH)
            last_sum = h1_ps[(NOH - 1) % 2]
            nc.scalar.activation(vecs[:, :, NOH], last_sum[:, 0:P], ACT.Copy).then_inc(vecs_fixed, 1)
            nc.scalar.activation(fixed[:, NOH, :], last_sum[:, 0:BATCH], ACT.Copy).then_inc(fixed_ready, 1)
            act.wait_ge(weights_in, 6 * 16)
            with act.Fori(1, TILES) as t:
                act.wait_ge(gram_done, t)
                move_group(t, 0)
                move_group(t, 1)
                near_pairs(t - 1)
                act.wait_ge(fixed_ready, NOH)
                move_fixed(t)
                for i in range(2, GROUPS - 1):
                    move_group(t, i)
                relu_h1a(t - 1)
                move_group(t, GROUPS - 1)
                relu_h2(t - 1)
            near_pairs(TILES - 1)
            relu_h1a(TILES - 1)
            relu_h2(TILES - 1)
            act.wait_ge(y_done, 1)
            nc.scalar.activation(y_sb[:], y_ps, ACT.Copy).then_inc(y_ready, 1)

        @block.vector
        def _(dve):
            nc.vector.memset(gram_ps[:], 0.0).then_inc(gram_cleared, 1)
            for j in range(NOH):
                dve.wait_ge(bc_in[j], 16)
                dve.wait_ge(rows_in, 16)
                if j >= 2:
                    dve.wait_ge(looked_up, j - 1)
                for c in range(DVE_CH[j]):
                    nc.vector.tensor_scalar(onehot[:, j % 2, c, :], ids_bc[:, j, :], rows_sb[:, c:c + 1], None,
                                            ALU.is_equal).then_inc(oh_dve, 1)
                    if c == 3:
                        dve.wait_ge(hi_ready, j + 1)
                        nc.vector.tensor_tensor(lo[:, j % 2].rearrange("p c d -> p (c d)"), raw[:, j % 2, :],
                                                hi[:, j % 2].rearrange("p c d -> p (c d)"),
                                                ALU.subtract).then_inc(lo_ready, 1)
            dve.wait_ge(weights_in, 6 * 16)
            nc.vector.tensor_tensor(w1s_sb[:], w1d_sb[:, 0, :], w1d_sb[:, 1, :], ALU.add).then_inc(w1_summed, 1)

            def pair_products(t):
                later = not (isinstance(t, int) and t == 0)
                dve.wait_ge(gram_done, t + 1)
                if later:
                    dve.wait_ge(near_ready, t)
                    dve.wait_ge(pairs_ready, t)
                nc.vector.transpose(zfull[:, 0:SLOTS, :], gram_ps[:, :, 0:SLOTS].rearrange("q b g -> q g b")
                                    ).then_inc(z_ready, 1)
                nc.vector.transpose(zfull[:, SLOTS:, :], gram_ps[:, :, 0:HALF].rearrange("q b g -> q g b")
                                    ).then_inc(z_ready, 1)
                dve.wait_ge(z_ready, 2 * t + 2)
                if later:
                    dve.wait_ge(zt_done, t)
                nc.vector.tensor_copy(pairs[:, NEAR:, :], walk(NEAR, SLOTS)).then_inc(pairs_ready, 1)

            def zt_copy(t):
                dve.wait_ge(zt_done, t + 1)
                if not (isinstance(t, int) and t == 0):
                    dve.wait_ge(h1_done, 2 * t)
                nc.vector.tensor_copy(zt[:].rearrange("k c b -> k (c b)"), zt_ps[0:ZK, 0:ZCH * P]
                                      ).then_inc(zt_ready, 1)

            def relu_h1b(t):
                dve.wait_ge(h1_done, 2 * t + 2)
                if not (isinstance(t, int) and t == 0):
                    dve.wait_ge(h2_done, NT2 * t)
                for n in range(NT1 // 2, NT1):
                    m = n - NT1 // 2
                    nc.vector.tensor_scalar(h1[:, n, :], h1_ps[1][:, m * P:(m + 1) * P], b1_sb[:, n:n + 1], 0.0,
                                            ALU.add, ALU.max).then_inc(h1b_ready, 1)

            def relu_h2_far(t):
                dve.wait_ge(h2_done, NT2 * t + 2)
                nc.vector.tensor_scalar(h2[:, 1, bass.ds(t * P, P)], h2_at[1], b2_sb[:, 1:2], 0.0, ALU.add, ALU.max
                                        ).then_inc(h2_far_ready, 1)

            pair_products(0)
            zt_copy(0)
            relu_h1b(0)
            with dve.Fori(1, TILES) as t:
                pair_products(t)
                relu_h2_far(t - 1)
                zt_copy(t)
                relu_h1b(t)
            relu_h2_far(TILES - 1)

        @block.tensor
        def _(pe):
            def look_up(j):
                if j >= 2:
                    pe.wait_ge(fixed_ready, j - 1)
                for c in range(OH_CH):
                    if c < DVE_CH[j]:
                        pe.wait_ge(oh_dve, sum(DVE_CH[:j]) + c + 1)
                    else:
                        pe.wait_ge(oh_act, sum(OH_CH - m for m in DVE_CH[:j]) + c - DVE_CH[j] + 1)
                    if c == 0:
                        pe.wait_ge(hi_ready, j + 1)
                    nc.tensor.matmul(h1_ps[j % 2][:, 0:BATCH], hi[:, j % 2, c, :], onehot[:, j % 2, c, :],
                                     start=(c == 0), stop=False)
                pe.wait_ge(lo_ready, j + 1)
                for c in range(OH_CH):
                    last = nc.tensor.matmul(h1_ps[j % 2][:, 0:BATCH], lo[:, j % 2, c, :], onehot[:, j % 2, c, :],
                                            start=False, stop=(c == OH_CH - 1))
                last.then_inc(looked_up, 1)

            def turn_group(t, i):
                pe.wait_ge(gathered[i], 16 * GROUP[i] * t + 16 * GROUP[i])
                if not (isinstance(t, int) and t == 0 and i < 2):
                    pe.wait_ge(vecs_moved, GROUPS * t + i - 1)
                for k in range(GROUP[i]):
                    last = nc.tensor.transpose(turn_ps[i % 2][:, k * P:(k + 1) * P], got[:, GROUP_AT[i] + k, :],
                                               ident_sb[:])
                last.then_inc(turned, 1)

            def gram(t):
                pe.wait_ge(vecs_fixed, t + 2)
                pe.wait_ge(vecs_moved, GROUPS * t + GROUPS)
                if not (isinstance(t, int) and t == 0):
                    pe.wait_ge(z_ready, 2 * t)
                for b in range(BLK):
                    for j in range(QUADS):
                        v = vecs[:, BLK * j + b, 0:SLOTS]
                        last = nc.tensor.matmul(gram_ps[BLK * j:BLK * j + SLOTS, b, 0:SLOTS], v, v,
                                                start=True, stop=True)
                last.then_inc(gram_done, 1)

            def turn_pairs(t):
                pe.wait_ge(near_ready, t + 1)
                if not (isinstance(t, int) and t == 0):
                    pe.wait_ge(zt_ready, t)
                for c in range(ZCH):
                    if ZF * (c + 1) > NEAR >= ZF * c:
                        pe.wait_ge(pairs_ready, t + 1)
                    last = nc.tensor.transpose(zt_ps[0:ZK, c * P:(c + 1) * P],
                                               pairs[:, ZF * c:ZF * (c + 1), :].rearrange("b f s -> b (f s)"),
                                               ident_sb[:])
                last.then_inc(zt_done, 1)

            def layer1_dense(t):
                for n in range(NT1):
                    bank, col = h1_ps[n // 2], (n % 2) * P
                    if n % 2 == 0 and not (isinstance(t, int) and t == 0):
                        pe.wait_ge(h1a_ready if n == 0 else h1b_ready, NT1 // 2 * t)
                        if n == 0:
                            pe.wait_ge(h2_far_ready, t)
                    nc.tensor.matmul(bank[:, col:col + P], w1s_sb[:, n * P:(n + 1) * P],
                                     fixed[:, 0, bass.ds(t * P, P)], start=(n % 2 == 0), stop=False,
                                     skip_group_check=True)

            def layer1_pairs(t, parts):
                pe.wait_ge(zt_ready, t + 1)
                for n in parts:
                    bank, col = h1_ps[n // 2], (n % 2) * P
                    for c in range(ZCH):
                        last = nc.tensor.matmul(bank[:, col:col + P], w1p_sb[:, c, n * P:(n + 1) * P], zt[:, c, :],
                                                start=False, stop=(c == ZCH - 1), skip_group_check=True)
                    if n % 2 == 1:
                        last.then_inc(h1_done, 1)

            def layer2(t):
                if not (isinstance(t, int) and t == 0):
                    pe.wait_ge(h2_ready, t)
                for m in range(NT2):
                    for n in range(NT1):
                        if m == 0:
                            half = NT1 // 2
                            pe.wait_ge(h1a_ready if n < half else h1b_ready, half * t + n % half + 1)
                        last = nc.tensor.matmul(h2_at[m], w2_sb[:, n, m * P:(m + 1) * P],
                                                h1[:, n, :], start=(n == 0), stop=(n == NT1 - 1))
                    last.then_inc(h2_done, 1)

            def layer3(t):
                pe.wait_ge(h2_ready, t + 1)
                pe.wait_ge(h2_far_ready, t + 1)
                for m in range(NT2):
                    last = nc.tensor.matmul(y_ps[:, t:t + 1], h2[:, m, t * P:(t + 1) * P], w3_sb[:, m:m + 1],
                                            start=(m == 0), stop=(m == NT2 - 1))
                if t == TILES - 1:
                    last.then_inc(y_done, 1)

            early = {1: [(0, 0)], 2: [(0, 1)], 3: [(0, 2)], 4: [(0, 3)], 5: [(0, 4)], 6: [(0, 5), (1, 0)], 7: [(1, 1)]}
            for j in range(NOH):
                look_up(j)
                if j == 0:
                    pe.wait_ge(ident_in, 16)
                for t, i in early.get(j, []):
                    turn_group(t, i)
            pe.wait_ge(gram_cleared, 1)
            gram(0)
            pe.wait_ge(weights_in, 6 * 16)
            pe.wait_ge(w1_summed, 1)
            with pe.Fori(1, TILES) as t:
                turn_group(t, 2)
                turn_pairs(t - 1)
                turn_group(t, 3)
                layer1_dense(t - 1)
                turn_group(t, 4)
                layer1_pairs(t - 1, range(NT1 - 1))
                turn_group(t, 5)
                layer1_pairs(t - 1, [NT1 - 1])
                gram(t)
                layer2(t - 1)
                with pe.If(t < TILES - 1):
                    turn_group(t + 1, 0)
                    turn_group(t + 1, 1)
            turn_pairs(TILES - 1)
            layer1_dense(TILES - 1)
            layer1_pairs(TILES - 1, range(NT1))
            for t in range(TILES - 2):
                layer3(t)
            layer2(TILES - 1)
            layer3(TILES - 2)
            layer3(TILES - 1)


def kernel(**inputs):
    import concourse.bacc as bacc
    from concourse.bass_utils import run_bass_kernel_spmd

    a = {k: np.asarray(v) for k, v in inputs.items()}
    ids = a["ids"]
    w1 = a["W_top1"]
    row_of = (OH_CH * np.arange(OH_PART)[:, None] + np.arange(OH_CH)[None, :]).astype(np.float32)
    rows = np.concatenate([row_of, -row_of, np.ones((OH_PART, 1), np.float32)], axis=1)
    arrays = {
        "ids": ids.reshape(P, TILES * FIELDS),
        "ids_oh": np.stack([ids[:, f].reshape(P, TILES).T.reshape(BATCH) for f in ONEHOT]),
        "dense_t": a["r_dense_features"].reshape(P, TILES, DIM).transpose(2, 1, 0).reshape(DIM, BATCH),
        "oh_tables": np.stack([a[f"tbl_{f}"].reshape(OH_PART, OH_CH * DIM) for f in ONEHOT]),
        "w1_pairs": w1[w1_pair_rows()].reshape(ZCH, ZK, H1).transpose(1, 0, 2),
        "w1_dense": np.stack([w1[:DIM], w1[-DIM:]], axis=1),
        "w2": a["W_top2"].reshape(NT1, P, H2).transpose(1, 0, 2),
        "w3": a["W_top3"].reshape(NT2, P).T,
        "b1": a["b_top1"].reshape(NT1, P).T,
        "b2": a["b_top2"].reshape(NT2, P).T,
        "ident": np.eye(P, dtype=np.float32),
        "rows": rows,
    }
    for f in GATHERED:
        arrays[f"tbl_{f}"] = a[f"tbl_{f}"]
    arrays = {k: np.ascontiguousarray(v) for k, v in arrays.items()}

    nc = bacc.Bacc("TRN2", target_bir_lowering=False, num_devices=1)
    d = {k: nc.dram_tensor(k, v.shape, mybir.dt.from_np(v.dtype), kind="ExternalInput").ap()
         for k, v in arrays.items()}
    y = nc.dram_tensor("y", (BATCH, 1), F32, kind="ExternalOutput").ap()
    dlrm_tower(nc, d["ids"], d["ids_oh"], d["dense_t"], [d["oh_tables"][j] for j in range(NOH)],
               [d[f"tbl_{f}"] for f in GATHERED], d["w1_pairs"], d["w1_dense"], d["w2"], d["w3"],
               d["b1"], d["b2"], d["ident"], d["rows"], y.rearrange("(p t) o -> p (t o)", t=TILES))
    r = run_bass_kernel_spmd(nc, [arrays], core_ids=[0])
    return r.results[0]["y"]
```

```python
from contextlib import ExitStack

import numpy as np

import concourse.bass as bass
from concourse import mybir

F32 = mybir.dt.float32
F32R = mybir.dt.float32r
I32 = mybir.dt.int32
ALU = mybir.AluOpType
ACT = mybir.ActivationFunctionType

P = 128
BATCH, DIM, FIELDS = 512, 128, 26
TILES = BATCH // P
SLOTS = FIELDS + 1
HALF = (SLOTS - 1) // 2
H1, H2 = 512, 256

ONEHOT = [2, 4, 6, 13, 14, 17, 18, 23, 24]
GATHERED = [f for f in range(FIELDS) if f not in ONEHOT]
NOH = len(ONEHOT)
FIXED = 1 + NOH
OH_ROWS = 1000
OH_PART = 125
OH_CH = OH_ROWS // OH_PART
OH_HALF = OH_CH * DIM // 2
OH_SPLIT = BATCH // 2
DVE_CH = [OH_CH - 1 - j % 2 for j in range(NOH)]
GROUP = [3, 3, 3, 3, 3, 2]
GROUPS = len(GROUP)
TURN_BANKS = 3
GROUP_AT = [sum(GROUP[:i]) for i in range(GROUPS + 1)]
assert GROUP_AT[-1] == len(GATHERED) and GROUPS % TURN_BANKS == 0 and GROUPS <= NOH - 2 and SLOTS % 2 == 1

NEAR = SLOTS - HALF
ZCH = 3
ZF = SLOTS // ZCH
ZK = ZF * HALF
AHEAD = ZF + HALF
ETS = SLOTS + 1
BLK = 32
QUADS = P // BLK
NT1, NT2 = H1 // P, H2 // P


def slot_fields():
    return [0] + [1 + f for f in ONEHOT] + [1 + f for f in GATHERED]


def w1_pair_rows():
    of = slot_fields()
    rows = []
    for f in range(SLOTS):
        for step in range(1, HALF + 1):
            a, b = sorted((of[f], of[(f + step) % SLOTS]))
            if a == 0:
                rows.append(DIM + b - 1)
            else:
                i, j = a - 1, b - 1
                rows.append(DIM + FIELDS + i * FIELDS - i * (i + 1) // 2 + j - i - 1)
    return rows


def dlrm_tower(nc, ids, ids_oh, dense_t, oh_tables, tables, w1_pairs, w1_dense, w2, w3, b1, b2, ident, rows, out):
    ctx = ExitStack()
    with ctx:
        def sb(name, shape, dt=F32):
            return ctx.enter_context(nc.sbuf_tensor(name, shape, dt))

        def psum(name, shape):
            return ctx.enter_context(nc.psum_tensor(name, shape, F32))

        def sem(name):
            return ctx.enter_context(nc.semaphore(name))

        ids_sb = sb("ids_sb", [P, TILES * FIELDS], I32)
        ids_bc = sb("ids_bc", [OH_PART, NOH, BATCH], I32)
        ident_sb = sb("ident_sb", [P, P])
        rows_sb = sb("rows_sb", [OH_PART, 2 * OH_CH + 1])
        raw = sb("raw", [OH_PART, 2, OH_CH * DIM])
        hi = sb("hi", [OH_PART, 2, OH_CH, DIM], F32R)
        lo = sb("lo", [OH_PART, 2, OH_CH, DIM], F32R)
        onehot = sb("onehot", [OH_PART, 2, OH_CH, BATCH], F32R)
        dist = sb("dist", [OH_PART, BATCH])
        fixed = sb("fixed", [P, FIXED, BATCH])
        got = sb("got", [P, len(GATHERED), DIM])
        vecs = sb("vecs", [P, P, ETS])
        zfull = sb("zfull", [P, SLOTS + HALF, BLK])
        pairs = sb("pairs", [P, SLOTS, HALF])
        zt = sb("zt", [ZK, ZCH, P])
        w1p_sb = sb("w1p_sb", [ZK, ZCH, H1])
        w1d_sb = sb("w1d_sb", [P, 2, H1])
        w1s_sb = sb("w1s_sb", [P, H1])
        w2_sb = sb("w2_sb", [P, NT1, H2])
        w3_sb = sb("w3_sb", [P, NT2])
        b1_sb = sb("b1_sb", [P, NT1])
        b2_sb = sb("b2_sb", [P, NT2])
        h1 = sb("h1", [P, NT1, P])
        h2 = sb("h2", [P, NT2, BATCH])
        y_sb = sb("y_sb", [P, TILES])

        turn_ps = [psum(f"turn_ps{i}", [P, 512]) for i in range(TURN_BANKS)]
        gram_ps = psum("gram_ps", [P, BLK, BLK])
        zt_ps = psum("zt_ps", [P, 512])
        h1_ps = [psum(f"h1_ps{i}", [P, 512]) for i in range(2)]
        h2_at = [h1_ps[m][:, 0:P] for m in range(NT2)]

        def turn_bank(t, i):
            return zt_ps if isinstance(t, int) and t == 1 and i == 3 else turn_ps[i % TURN_BANKS]

        y_ps = zt_ps[:, ZCH * P:ZCH * P + TILES]

        ids_in = sem("ids_in")
        rows_in = sem("rows_in")
        bc_in = [sem(f"bc_in{j}") for j in range(NOH)]
        table_in = [sem(f"table_in{i}") for i in range(2)]
        table0_in = [sem(f"table0_in{i}") for i in range(2)]
        ident_in = sem("ident_in")
        dense_in = sem("dense_in")
        weights_in = sem("weights_in")
        gathered = [sem(f"gathered{i}") for i in range(GROUPS)]
        hi_ready = sem("hi_ready")
        lo_ready = sem("lo_ready")
        oh_dve = sem("oh_dve")
        dist_ready = sem("dist_ready")
        oh_act = sem("oh_act")
        looked_up = sem("looked_up")
        fixed_ready = sem("fixed_ready")
        last_fixed = sem("last_fixed")
        turned = sem("turned")
        vecs_fixed = sem("vecs_fixed")
        vecs_moved = sem("vecs_moved")
        gram_cleared = sem("gram_cleared")
        gram_done = sem("gram_done")
        z_ready = sem("z_ready")
        near_ready = sem("near_ready")
        pairs_ready = sem("pairs_ready")
        zt_done = sem("zt_done")
        zt_ready = sem("zt_ready")
        zt0_ready = sem("zt0_ready")
        w1_summed = sem("w1_summed")
        h1_done = sem("h1_done")
        h1a_ready = sem("h1a_ready")
        h1b_ready = sem("h1b_ready")
        h2_done = sem("h2_done")
        h2_ready = sem("h2_ready")
        h2_far_ready = sem("h2_far_ready")
        y_done = sem("y_done")
        y_ready = sem("y_ready")
        out_done = sem("out_done")

        zt0_ps = turn_ps[0][0:ZK, 0:P]

        def walk(f0, f1):
            z = zfull[:]
            return bass.AP(z.tensor, z.offset + BLK + (BLK + 1) * f0, [z.ap[0], [BLK + 1, f1 - f0], [BLK, HALF]])

        block = ctx.enter_context(nc.Block())

        @block.sync
        def _(sp):
            sp.dma_start(ids_sb[:], ids).then_inc(ids_in, 16)
            sp.dma_start(rows_sb[:], rows).then_inc(rows_in, 16)
            for j in range(NOH):
                if j >= 2:
                    sp.wait_ge(lo_ready, j - 1)
                if j >= 1:
                    sp.dma_start(ids_bc[:, j, :], ids_oh[j:j + 1, :].to_broadcast([OH_PART, BATCH])).then_inc(bc_in[j], 16)
                    sp.dma_start(raw[:, j % 2, :], oh_tables[j]).then_inc(table_in[j % 2], 16)
                if j == 1:
                    sp.dma_start(ident_sb[:], ident).then_inc(ident_in, 16)
            sp.dma_start(fixed[:, 0, :], dense_t).then_inc(dense_in, 16)
            for there, here in ((w1p_sb, w1_pairs), (w1d_sb, w1_dense), (w2_sb, w2), (w3_sb, w3), (b1_sb, b1), (b2_sb, b2)):
                sp.dma_start(there[:], here).then_inc(weights_in, 16)
            sp.wait_ge(y_ready, 1)
            sp.dma_start(out, y_sb[:]).then_inc(out_done, 16)
            sp.wait_ge(out_done, 16)

        @block.gpsimd
        def _(pool):
            pool.wait_ge(ids_in, 16)
            for t in range(TILES):
                for i in range(GROUPS):
                    if t > 0:
                        pool.wait_ge(turned, GROUPS * (t - 1) + i + 1)
                    for k in range(GROUP_AT[i], GROUP_AT[i + 1]):
                        at = t * FIELDS + GATHERED[k]
                        nc.gpsimd.indirect_dma_start(
                            out=got[:, k, :], out_offset=None, in_=tables[k],
                            in_offset=bass.IndirectOffsetOnAxis(ap=ids_sb[:, at:at + 1], axis=0),
                        ).then_inc(gathered[i], 16)

        @block.scalar
        def _(act):
            act.dma_start(ids_bc[:, 0, :], ids_oh[0:1, :].to_broadcast([OH_PART, BATCH])).then_inc(bc_in[0], 16)
            for half in range(2):
                act.dma_start(raw[:, 0, half * OH_HALF:(half + 1) * OH_HALF],
                              oh_tables[0][:, half * OH_HALF:(half + 1) * OH_HALF]).then_inc(table0_in[half], 16)

            def look_up(j):
                if j < NOH:
                    if j > 0:
                        act.wait_ge(table_in[j % 2], 16 * ((j + 1) // 2))
                    if j >= 2:
                        act.wait_ge(looked_up, j - 1)
                    for half in range(2 if j == 0 else 1):
                        c0, c1 = (half * OH_CH // 2, (half + 1) * OH_CH // 2) if j == 0 else (0, OH_CH)
                        if j == 0:
                            act.wait_ge(table0_in[half], 16)
                        nc.scalar.activation(hi[:, j % 2, c0:c1].rearrange("p c d -> p (c d)"),
                                             raw[:, j % 2, c0 * DIM:c1 * DIM], ACT.Copy).then_inc(hi_ready, 1)
                    act.wait_ge(bc_in[j], 16)
                    act.wait_ge(rows_in, 16)
                    for c in range(DVE_CH[j], OH_CH):
                        n = sum(OH_CH - m for m in DVE_CH[:j]) + c - DVE_CH[j]
                        if n > 0:
                            act.wait_ge(oh_act, n)
                        nc.scalar.activation(dist[:], ids_bc[:, j, :], ACT.Square,
                                             bias=rows_sb[:, OH_CH + c:OH_CH + c + 1]).then_inc(dist_ready, 1)
                        act.wait_ge(dist_ready, n + 1)
                        nc.scalar.activation(onehot[:, j % 2, c, :], dist[:], ACT.Relu,
                                             bias=rows_sb[:, 2 * OH_CH:], scale=-1.0).then_inc(oh_act, 1)
                if j >= 1:
                    act.wait_ge(looked_up, j)
                    nc.scalar.activation(fixed[:, j, :], h1_ps[(j - 1) % 2][:, 0:BATCH],
                                         ACT.Copy).then_inc(fixed_ready, 1)

            def move_group(t, i):
                act.wait_ge(turned, GROUPS * t + i + 1)
                nc.scalar.activation(
                    vecs[:, :, FIXED + GROUP_AT[i]:FIXED + GROUP_AT[i + 1]].rearrange("d b s -> d s b"),
                    turn_bank(t, i)[:, 0:GROUP[i] * P].rearrange("d (s b) -> d s b", s=GROUP[i]),
                    ACT.Copy).then_inc(vecs_moved, 1)

            def move_fixed(t):
                nc.scalar.activation(vecs[:, :, 0:FIXED].rearrange("d b s -> d s b"),
                                     fixed[:, :, bass.ds(t * P, P)], ACT.Copy).then_inc(vecs_fixed, 1)

            def relu_h1a(t):
                act.wait_ge(h1_done, 2 * t + 1)
                for n in range(NT1 // 2):
                    nc.scalar.activation(h1[:, n, :], h1_ps[0][:, n * P:(n + 1) * P], ACT.Relu,
                                         bias=b1_sb[:, n:n + 1]).then_inc(h1a_ready, 1)

            def relu_h2(t):
                act.wait_ge(h2_done, NT2 * t + 1)
                nc.scalar.activation(h2[:, 0, bass.ds(t * P, P)], h2_at[0], ACT.Relu, bias=b2_sb[:, 0:1]).then_inc(h2_ready, 1)

            def near_pairs(t):
                act.wait_ge(z_ready, 2 * t + 1)
                nc.scalar.activation(pairs[:, 0:NEAR, :], walk(0, NEAR), ACT.Copy).then_inc(near_ready, 1)

            for j in range(NOH):
                look_up(j)
                if 2 <= j < GROUPS + 2:
                    move_group(0, j - 2)
            act.wait_ge(fixed_ready, NOH - 1)
            act.wait_ge(dense_in, 16)
            nc.scalar.activation(vecs[:, :, 0:NOH].rearrange("d b s -> d s b"), fixed[:, 0:NOH, 0:P],
                                 ACT.Copy).then_inc(vecs_fixed, 1)
            act.wait_ge(weights_in, 6 * 16)
            act.wait_ge(gram_done, 1)
            for i in range(4):
                move_group(1, i)
            near_pairs(0)
            act.wait_ge(looked_up, NOH + 1)
            nc.scalar.activation(fixed[:, NOH, OH_SPLIT:], h1_ps[NOH % 2][:, 0:BATCH - OH_SPLIT],
                                 ACT.Copy).then_inc(fixed_ready, 1)
            act.wait_ge(fixed_ready, NOH)
            act.wait_ge(last_fixed, 1)
            with act.Fori(1, TILES - 1) as t:
                move_fixed(t)
                move_group(t, 4)
                relu_h1a(t - 1)
                move_group(t, 5)
                relu_h2(t - 1)
                near_pairs(t)
                act.wait_ge(gram_done, t + 1)
                for i in range(4):
                    move_group(t + 1, i)
            move_fixed(TILES - 1)
            relu_h1a(TILES - 2)
            move_group(TILES - 1, 4)
            move_group(TILES - 1, 5)
            relu_h2(TILES - 2)
            act.wait_ge(z_ready, 2 * (TILES - 1) + 1)
            nc.scalar.activation(pairs[:, 0:ZF, :], walk(0, ZF), ACT.Copy).then_inc(near_ready, 1)
            act.wait_ge(z_ready, 2 * (TILES - 1) + 2)
            nc.scalar.activation(pairs[:, ZF:NEAR, :], walk(ZF, NEAR), ACT.Copy).then_inc(near_ready, 1)
            act.wait_ge(zt_done, TILES)
            act.wait_ge(h1_done, 2 * (TILES - 1))
            nc.scalar.activation(zt[:, 0, :], zt0_ps, ACT.Copy).then_inc(zt0_ready, 1)
            relu_h1a(TILES - 1)
            relu_h2(TILES - 1)
            act.wait_ge(y_done, 1)
            nc.scalar.activation(y_sb[:], y_ps, ACT.Copy).then_inc(y_ready, 1)

        @block.vector
        def _(dve):
            nc.vector.memset(gram_ps[:], 0.0).then_inc(gram_cleared, 1)
            for j in range(NOH):
                dve.wait_ge(bc_in[j], 16)
                dve.wait_ge(rows_in, 16)
                if j >= 2:
                    dve.wait_ge(looked_up, j - 1)
                for c in range(DVE_CH[j]):
                    nc.vector.tensor_scalar(onehot[:, j % 2, c, :], ids_bc[:, j, :], rows_sb[:, c:c + 1], None,
                                            ALU.is_equal).then_inc(oh_dve, 1)
                    if c == (3 if j > 0 else DVE_CH[0] - 1):
                        dve.wait_ge(hi_ready, j + 2)
                        nc.vector.tensor_tensor(lo[:, j % 2].rearrange("p c d -> p (c d)"), raw[:, j % 2, :],
                                                hi[:, j % 2].rearrange("p c d -> p (c d)"),
                                                ALU.subtract).then_inc(lo_ready, 1)
            dve.wait_ge(looked_up, NOH)
            last_sums = h1_ps[(NOH - 1) % 2]
            nc.vector.tensor_copy(vecs[:, :, NOH], last_sums[:, 0:P]).then_inc(vecs_fixed, 1)
            nc.vector.tensor_copy(fixed[:, NOH, P:OH_SPLIT], last_sums[:, P:OH_SPLIT]).then_inc(last_fixed, 1)
            dve.wait_ge(weights_in, 6 * 16)
            nc.vector.tensor_tensor(w1s_sb[:], w1d_sb[:, 0, :], w1d_sb[:, 1, :], ALU.add).then_inc(w1_summed, 1)

            def pair_products(t):
                later = not (isinstance(t, int) and t == 0)
                dve.wait_ge(gram_done, t + 1)
                if later:
                    dve.wait_ge(near_ready, t)
                    dve.wait_ge(pairs_ready, t)
                nc.vector.transpose(zfull[:, 0:SLOTS, :], gram_ps[:, :, 0:SLOTS].rearrange("q b g -> q g b")
                                    ).then_inc(z_ready, 1)
                nc.vector.transpose(zfull[:, SLOTS:, :], gram_ps[:, :, 0:HALF].rearrange("q b g -> q g b")
                                    ).then_inc(z_ready, 1)
                dve.wait_ge(z_ready, 2 * t + 2)
                if later:
                    dve.wait_ge(zt_done, t)
                nc.vector.tensor_copy(pairs[:, NEAR:, :], walk(NEAR, SLOTS)).then_inc(pairs_ready, 1)

            def zt_copy(t):
                dve.wait_ge(zt_done, t + 1)
                if not (isinstance(t, int) and t == 0):
                    dve.wait_ge(h1_done, 2 * t)
                nc.vector.tensor_copy(zt[:].rearrange("k c b -> k (c b)"), zt_ps[0:ZK, 0:ZCH * P]
                                      ).then_inc(zt_ready, 1)

            def relu_h1b(t):
                dve.wait_ge(h1_done, 2 * t + 2)
                if not (isinstance(t, int) and t == 0):
                    dve.wait_ge(h2_done, NT2 * t)
                for n in range(NT1 // 2, NT1):
                    m = n - NT1 // 2
                    nc.vector.tensor_scalar(h1[:, n, :], h1_ps[1][:, m * P:(m + 1) * P], b1_sb[:, n:n + 1], 0.0,
                                            ALU.add, ALU.max).then_inc(h1b_ready, 1)

            def relu_h2_far(t):
                dve.wait_ge(h2_done, NT2 * t + 2)
                nc.vector.tensor_scalar(h2[:, 1, bass.ds(t * P, P)], h2_at[1], b2_sb[:, 1:2], 0.0, ALU.add, ALU.max
                                        ).then_inc(h2_far_ready, 1)

            pair_products(0)
            zt_copy(0)
            relu_h1b(0)
            with dve.Fori(1, TILES - 1) as t:
                pair_products(t)
                relu_h2_far(t - 1)
                zt_copy(t)
                relu_h1b(t)
            dve.wait_ge(gram_done, TILES)
            dve.wait_ge(near_ready, TILES - 1)
            dve.wait_ge(pairs_ready, TILES - 1)
            for row, g0, g1 in ((0, 0, AHEAD), (AHEAD, AHEAD, SLOTS), (SLOTS, 0, HALF)):
                if row == SLOTS:
                    relu_h2_far(TILES - 2)
                nc.vector.transpose(zfull[:, row:row + g1 - g0, :], gram_ps[:, :, g0:g1].rearrange("q b g -> q g b")
                                    ).then_inc(z_ready, 1)
            dve.wait_ge(z_ready, 2 * (TILES - 1) + 3)
            dve.wait_ge(zt_done, TILES - 1)
            nc.vector.tensor_copy(pairs[:, NEAR:, :], walk(NEAR, SLOTS)).then_inc(pairs_ready, 1)
            dve.wait_ge(zt_done, TILES + 1)
            nc.vector.tensor_copy(zt[:, 1:, :].rearrange("k c b -> k (c b)"), zt_ps[0:ZK, P:ZCH * P]).then_inc(zt_ready, 1)
            relu_h1b(TILES - 1)
            relu_h2_far(TILES - 1)

        @block.tensor
        def _(pe):
            def look_up(j, bank, b0, b1):
                for c in range(OH_CH):
                    if c < DVE_CH[j]:
                        pe.wait_ge(oh_dve, sum(DVE_CH[:j]) + c + 1)
                    else:
                        pe.wait_ge(oh_act, sum(OH_CH - m for m in DVE_CH[:j]) + c - DVE_CH[j] + 1)
                    if c == 0:
                        pe.wait_ge(hi_ready, j + 2 if j > 0 else 1)
                    if j == 0 and c == OH_CH // 2:
                        pe.wait_ge(hi_ready, 2)
                    nc.tensor.matmul(bank[:, 0:b1 - b0], hi[:, j % 2, c, :], onehot[:, j % 2, c, b0:b1],
                                     start=(c == 0), stop=False)
                pe.wait_ge(lo_ready, j + 1)
                for c in range(OH_CH):
                    last = nc.tensor.matmul(bank[:, 0:b1 - b0], lo[:, j % 2, c, :], onehot[:, j % 2, c, b0:b1],
                                            start=False, stop=(c == OH_CH - 1))
                last.then_inc(looked_up, 1)

            def turn_group(t, i):
                pe.wait_ge(gathered[i], 16 * GROUP[i] * t + 16 * GROUP[i])
                if not (isinstance(t, int) and (t == 0 and i < TURN_BANKS or t == 1 and i == 3)):
                    pe.wait_ge(vecs_moved, GROUPS * t + i + 1 - TURN_BANKS)
                for k in range(GROUP[i]):
                    last = nc.tensor.transpose(turn_bank(t, i)[:, k * P:(k + 1) * P], got[:, GROUP_AT[i] + k, :],
                                               ident_sb[:])
                last.then_inc(turned, 1)

            def gram(t):
                pe.wait_ge(vecs_fixed, t + 2)
                pe.wait_ge(vecs_moved, GROUPS * t + GROUPS)
                if not (isinstance(t, int) and t == 0):
                    pe.wait_ge(z_ready, 2 * t)
                for b in range(BLK):
                    for j in range(QUADS):
                        v = vecs[:, BLK * j + b, 0:SLOTS]
                        last = nc.tensor.matmul(gram_ps[BLK * j:BLK * j + SLOTS, b, 0:SLOTS], v, v,
                                                start=True, stop=True)
                last.then_inc(gram_done, 1)

            def turn_pairs(t, c0=0):
                pe.wait_ge(near_ready, t + 1 if c0 == 0 else t + 2)
                for c in range(c0, ZCH):
                    if ZF * (c + 1) > NEAR >= ZF * c:
                        pe.wait_ge(pairs_ready, t + 1)
                    last = nc.tensor.transpose(zt_ps[0:ZK, c * P:(c + 1) * P],
                                               pairs[:, ZF * c:ZF * (c + 1), :].rearrange("b f s -> b (f s)"),
                                               ident_sb[:])
                last.then_inc(zt_done, 1)

            def layer1_dense(t, parts=range(NT1)):
                for n in parts:
                    bank, col = h1_ps[n // 2], (n % 2) * P
                    nc.tensor.matmul(bank[:, col:col + P], w1s_sb[:, n * P:(n + 1) * P],
                                     fixed[:, 0, bass.ds(t * P, P)], start=(n % 2 == 0), stop=False,
                                     skip_group_check=True)

            def layer1_pairs(t, parts, c0=0):
                pe.wait_ge(zt_ready, t + 1)
                for n in parts:
                    bank, col = h1_ps[n // 2], (n % 2) * P
                    for c in range(c0, ZCH):
                        last = nc.tensor.matmul(bank[:, col:col + P], w1p_sb[:, c, n * P:(n + 1) * P], zt[:, c, :],
                                                start=False, stop=(c == ZCH - 1), skip_group_check=True)
                    if n % 2 == 1:
                        last.then_inc(h1_done, 1)

            def layer2(t, parts=range(NT2)):
                for m in parts:
                    for n in range(NT1):
                        if m == 0 and n == 0:
                            pe.wait_ge(h1a_ready, NT1 // 2 * (t + 1))
                        if m == 0 and n >= NT1 // 2:
                            pe.wait_ge(h1b_ready, NT1 // 2 * t + n - NT1 // 2 + 1)
                        last = nc.tensor.matmul(h2_at[m], w2_sb[:, n, m * P:(m + 1) * P],
                                                h1[:, n, :], start=(n == 0), stop=(n == NT1 - 1))
                    last.then_inc(h2_done, 1)

            def banks_free(t):
                pe.wait_ge(h2_ready, t + 1)
                pe.wait_ge(h2_far_ready, t + 1)

            def layer3(t):
                for m in range(NT2):
                    pe.wait_ge(h2_far_ready if m else h2_ready, t + 1)
                    last = nc.tensor.matmul(y_ps[:, t:t + 1], h2[:, m, t * P:(t + 1) * P], w3_sb[:, m:m + 1],
                                            start=(m == 0), stop=(m == NT2 - 1))
                if t == TILES - 1:
                    last.then_inc(y_done, 1)

            early = {1: [(0, 0)], 2: [(0, 1)], 3: [(0, 2)], 4: [(0, 3)], 5: [(0, 4)], 6: [(0, 5), (1, 0)], 7: [(1, 1), (1, 2)]}
            for j in range(NOH - 1):
                if j >= 2:
                    pe.wait_ge(fixed_ready, j - 1)
                look_up(j, h1_ps[j % 2], 0, BATCH)
                if j == 0:
                    pe.wait_ge(ident_in, 16)
                for t, i in early.get(j, []):
                    turn_group(t, i)
            pe.wait_ge(fixed_ready, NOH - 2)
            look_up(NOH - 1, h1_ps[(NOH - 1) % 2], 0, OH_SPLIT)
            turn_group(1, 3)
            pe.wait_ge(gram_cleared, 1)
            gram(0)
            pe.wait_ge(fixed_ready, NOH - 1)
            look_up(NOH - 1, h1_ps[NOH % 2], OH_SPLIT, BATCH)
            pe.wait_ge(vecs_moved, GROUPS + 4)
            turn_pairs(0)
            pe.wait_ge(weights_in, 6 * 16)
            pe.wait_ge(w1_summed, 1)
            pe.wait_ge(fixed_ready, NOH)
            pe.wait_ge(last_fixed, 1)
            layer1_dense(0)
            with pe.Fori(1, TILES - 1) as t:
                turn_group(t, 4)
                layer1_pairs(t - 1, range(NT1 - 1))
                turn_group(t, 5)
                layer1_pairs(t - 1, [NT1 - 1])
                turn_group(t + 1, 0)
                gram(t)
                turn_group(t + 1, 1)
                layer2(t - 1)
                turn_group(t + 1, 2)
                turn_pairs(t)
                turn_group(t + 1, 3)
                banks_free(t - 1)
                layer1_dense(t)
            layer1_pairs(TILES - 2, range(NT1))
            turn_group(TILES - 1, 4)
            layer3(0)
            layer2(TILES - 2, [0])
            turn_group(TILES - 1, 5)
            for t in range(1, TILES - 2):
                layer3(t)
            gram(TILES - 1)
            layer2(TILES - 2, [1])
            pe.wait_ge(h2_ready, TILES - 1)
            layer1_dense(TILES - 1, range(NT1 // 2))
            pe.wait_ge(near_ready, TILES)
            nc.tensor.transpose(zt0_ps, pairs[:, 0:ZF, :].rearrange("b f s -> b (f s)"), ident_sb[:]).then_inc(zt_done, 1)
            pe.wait_ge(h2_far_ready, TILES - 1)
            layer1_dense(TILES - 1, range(NT1 // 2, NT1))
            layer3(TILES - 2)
            turn_pairs(TILES - 1, 1)
            pe.wait_ge(zt0_ready, 1)
            for n in range(NT1):
                bank, col = h1_ps[n // 2], (n % 2) * P
                nc.tensor.matmul(bank[:, col:col + P], w1p_sb[:, 0, n * P:(n + 1) * P], zt[:, 0, :],
                                 start=False, stop=False, skip_group_check=True)
            layer1_pairs(TILES - 1, range(NT1), 1)
            layer2(TILES - 1)
            layer3(TILES - 1)


def kernel(**inputs):
    import concourse.bacc as bacc
    from concourse.bass_utils import run_bass_kernel_spmd

    a = {k: np.asarray(v) for k, v in inputs.items()}
    ids = a["ids"]
    w1 = a["W_top1"]
    row_of = (OH_CH * np.arange(OH_PART)[:, None] + np.arange(OH_CH)[None, :]).astype(np.float32)
    rows = np.concatenate([row_of, -row_of, np.ones((OH_PART, 1), np.float32)], axis=1)
    arrays = {
        "ids": ids.reshape(P, TILES * FIELDS),
        "ids_oh": np.stack([ids[:, f].reshape(P, TILES).T.reshape(BATCH) for f in ONEHOT]),
        "dense_t": a["r_dense_features"].reshape(P, TILES, DIM).transpose(2, 1, 0).reshape(DIM, BATCH),
        "oh_tables": np.stack([a[f"tbl_{f}"].reshape(OH_PART, OH_CH * DIM) for f in ONEHOT]),
        "w1_pairs": w1[w1_pair_rows()].reshape(ZCH, ZK, H1).transpose(1, 0, 2),
        "w1_dense": np.stack([w1[:DIM], w1[-DIM:]], axis=1),
        "w2": a["W_top2"].reshape(NT1, P, H2).transpose(1, 0, 2),
        "w3": a["W_top3"].reshape(NT2, P).T,
        "b1": a["b_top1"].reshape(NT1, P).T,
        "b2": a["b_top2"].reshape(NT2, P).T,
        "ident": np.eye(P, dtype=np.float32),
        "rows": rows,
    }
    for f in GATHERED:
        arrays[f"tbl_{f}"] = a[f"tbl_{f}"]
    arrays = {k: np.ascontiguousarray(v) for k, v in arrays.items()}

    nc = bacc.Bacc("TRN2", target_bir_lowering=False, num_devices=1)
    d = {k: nc.dram_tensor(k, v.shape, mybir.dt.from_np(v.dtype), kind="ExternalInput").ap()
         for k, v in arrays.items()}
    y = nc.dram_tensor("y", (BATCH, 1), F32, kind="ExternalOutput").ap()
    dlrm_tower(nc, d["ids"], d["ids_oh"], d["dense_t"], [d["oh_tables"][j] for j in range(NOH)],
               [d[f"tbl_{f}"] for f in GATHERED], d["w1_pairs"], d["w1_dense"], d["w2"], d["w3"],
               d["b1"], d["b2"], d["ident"], d["rows"], y.rearrange("(p t) o -> p (t o)", t=TILES))
    r = run_bass_kernel_spmd(nc, [arrays], core_ids=[0])
    return r.results[0]["y"]
```
